# Optimizing a Trainium2 kernel written in Bass

```python
import numpy as np
import jax
import jax.numpy as jnp

def _softmax(x, axis=-1):
    return jax.nn.softmax(x, axis=axis)

def _gelu(x):
    return jax.nn.gelu(x, approximate=True)

def _silu(x):
    return jax.nn.silu(x)

def _sigmoid(x):
    return jax.nn.sigmoid(x)

def _layernorm(x, axis=-1, eps=1e-05):
    m = jnp.mean(x, axis=axis, keepdims=True)
    v = jnp.var(x, axis=axis, keepdims=True)
    return (x - m) / jnp.sqrt(v + eps)

def _scatter_add(tgt, idx, src, axis=0):
    return tgt.at[idx].add(src)

def _segment_sum(src, seg, n):
    return jax.ops.segment_sum(src, seg, n)
kernel_name = 'mk_gnn_preln_d4_gnn_r16_031f81'

def setup_inputs(seed: int=0):
    np.random.seed(seed)
    _w = jnp.asarray

    def _rec_inputs():
        import jax
        import jax.numpy as jnp
        _gk = jax.random.key(seed)
        x = -0.0003713 + 1 * jax.random.normal(jax.random.fold_in(_gk, 1), (6250, 128), jnp.float32)
        src = jax.random.randint(jax.random.fold_in(_gk, 2), (100000,), 0, 6250, jnp.int32)
        dst = jnp.minimum((6250 * jax.random.uniform(jax.random.fold_in(_gk, 3), (100000,)) ** 2.0).astype(jnp.int32), 99999)
        _o = jnp.argsort(dst, stable=True)
        src = src[_o]
        dst = dst[_o]
        edge_attr_128 = 7.68618e-05 + 1.00005 * jax.random.normal(jax.random.fold_in(_gk, 11), (100000, 128), jnp.float32)
        return (x, src, dst, edge_attr_128)
    x, src, dst, edge_attr_128 = _rec_inputs()

    def _L0_gnn_setup():
        import jax, jax.numpy as jnp
        import numpy as np
        N_NODES = 6250
        N_EDGES = 100000
        D = 128
        K = 2
        ALPHA = 0.5

        def _appnp(x, edge_index):
            n = x.shape[0]
            loops = jnp.arange(n, dtype=edge_index.dtype)
            src = jnp.concatenate([edge_index[0], loops])
            dst = jnp.concatenate([edge_index[1], loops])
            ew = jnp.ones_like(src, dtype=x.dtype)
            deg = jax.ops.segment_sum(ew, dst, num_segments=n)
            dinv = jnp.where(deg > 0, jax.lax.rsqrt(deg), 0.0)
            norm = dinv[src] * ew * dinv[dst]
            h = x
            for _ in range(K):
                msg = norm[:, None] * x[src]
                agg = jax.ops.segment_sum(msg, dst, num_segments=n)
                x = (1.0 - ALPHA) * agg + ALPHA * h
            return x
        key = jax.random.key(seed)
        ks = jax.random.split(key, 5)
        x = jax.random.normal(ks[0], (N_NODES, D), dtype=jnp.float32)
        edge_index = jax.random.randint(ks[1], (2, N_EDGES), 0, N_NODES, dtype=jnp.int32)
        s = 1.0 / np.sqrt(D)
        w1 = jax.random.uniform(ks[2], (D, D), jnp.float32, -s, s)
        b1 = jnp.zeros((D,), jnp.float32)
        w2 = jax.random.uniform(ks[3], (D, D), jnp.float32, -s, s)
        b2 = jnp.zeros((D,), jnp.float32)
        return {'x': x, 'edge_index': edge_index, 'w1': w1, 'b1': b1, 'w2': w2, 'b2': b2}
    _L0_gnn_all = _L0_gnn_setup()
    _L0_gnn_in = {k: v for k, v in _L0_gnn_all.items() if k in ('w1', 'b1', 'w2', 'b2')}
    del _L0_gnn_all

    def _L1_gnn_setup():
        import jax, jax.numpy as jnp
        import numpy as np
        HIDDEN = 128
        HEADS = 8
        HEAD_DIM = HIDDEN // HEADS
        N_NODES = 3125
        N_EDGES = 31250
        key = jax.random.key(seed)
        ks = jax.random.split(key, 12)
        s = 1.0 / np.sqrt(HIDDEN)
        inp = {'edge_state': jax.random.normal(ks[0], (N_NODES, HIDDEN), jnp.float32), 'lg_edge_index': jax.random.randint(ks[1], (2, N_EDGES), 0, N_NODES, jnp.int64), 'angle_emb': jax.random.normal(ks[2], (N_EDGES, HIDDEN), jnp.float32), 'Wq': jax.random.normal(ks[3], (HIDDEN, HIDDEN), jnp.float32) * s, 'bq': jnp.zeros((HIDDEN,), jnp.float32), 'Wk': jax.random.normal(ks[4], (HIDDEN, HIDDEN), jnp.float32) * s, 'bk': jnp.zeros((HIDDEN,), jnp.float32), 'Wv': jax.random.normal(ks[5], (HIDDEN, HIDDEN), jnp.float32) * s, 'bv': jnp.zeros((HIDDEN,), jnp.float32), 'We': jax.random.normal(ks[6], (HIDDEN, HIDDEN), jnp.float32) * s, 'Wskip': jax.random.normal(ks[7], (HIDDEN, HIDDEN), jnp.float32) * s, 'bskip': jnp.zeros((HIDDEN,), jnp.float32), 'Wbeta': jax.random.normal(ks[8], (3 * HIDDEN, 1), jnp.float32) * s, 'ln_gamma': jnp.ones((HIDDEN,), jnp.float32), 'ln_beta': jnp.zeros((HIDDEN,), jnp.float32)}
        return inp
    _L1_gnn_all = _L1_gnn_setup()
    _L1_gnn_in = {k: v for k, v in _L1_gnn_all.items() if k in ('Wq', 'bq', 'Wk', 'bk', 'Wv', 'bv', 'We', 'Wskip', 'bskip', 'Wbeta', 'ln_gamma', 'ln_beta')}
    del _L1_gnn_all

    def _L2_gnn_setup():
        import jax, jax.numpy as jnp
        import numpy as np
        N = 6250
        E = 100000
        D_IN = 128
        D_H = 128
        D_OUT = 128
        key = jax.random.key(seed)
        ks = jax.random.split(key, 11)
        x = jax.random.normal(ks[0], (N, D_IN), dtype=jnp.float32)
        edge_index = jax.random.randint(ks[1], (2, E), 0, N, dtype=jnp.int32)
        s_in = 1.0 / np.sqrt(D_IN)
        s_h = 1.0 / np.sqrt(D_H)
        return {'x': x, 'edge_index': edge_index, 'W_neigh1': jax.random.uniform(ks[2], (D_H, D_IN), jnp.float32, -s_in, s_in), 'b_neigh1': jax.random.uniform(ks[3], (D_H,), jnp.float32, -s_in, s_in), 'W_self1': jax.random.uniform(ks[4], (D_H, D_IN), jnp.float32, -s_in, s_in), 'b_self1': jax.random.uniform(ks[5], (D_H,), jnp.float32, -s_in, s_in), 'W_neigh2': jax.random.uniform(ks[6], (D_OUT, D_H), jnp.float32, -s_h, s_h), 'b_neigh2': jax.random.uniform(ks[7], (D_OUT,), jnp.float32, -s_h, s_h), 'W_self2': jax.random.uniform(ks[8], (D_OUT, D_H), jnp.float32, -s_h, s_h), 'b_self2': jax.random.uniform(ks[9], (D_OUT,), jnp.float32, -s_h, s_h)}
    _L2_gnn_all = _L2_gnn_setup()
    _L2_gnn_in = {k: v for k, v in _L2_gnn_all.items() if k in ('W_neigh1', 'b_neigh1', 'W_self1', 'b_self1', 'W_neigh2', 'b_neigh2', 'W_self2', 'b_self2')}
    del _L2_gnn_all

    def _L3_gnn_setup():
        import jax, jax.numpy as jnp
        import numpy as np
        IN_C = 128
        OUT_C = 128
        N_NODES = 3125
        N_EDGES = 50000
        key = jax.random.key(seed)
        ks = jax.random.split(key, 10)
        s_in = 1.0 / np.sqrt(IN_C)
        s_in2 = 1.0 / np.sqrt(2 * IN_C)
        s_g = 1.0 / np.sqrt(3 * OUT_C)
        return {'x': jax.random.normal(ks[0], (N_NODES, IN_C), dtype=jnp.float32), 'edge_index': jax.random.randint(ks[1], (2, N_EDGES), 0, N_NODES, dtype=jnp.int64), 'W_src': jax.random.uniform(ks[2], (IN_C, OUT_C), jnp.float32, -s_in, s_in), 'b_src': jax.random.uniform(ks[3], (OUT_C,), jnp.float32, -s_in, s_in), 'W_dst': jax.random.uniform(ks[4], (IN_C, OUT_C), jnp.float32, -s_in, s_in), 'b_dst': jax.random.uniform(ks[5], (OUT_C,), jnp.float32, -s_in, s_in), 'W_edge': jax.random.uniform(ks[6], (2 * IN_C, OUT_C), jnp.float32, -s_in2, s_in2), 'b_edge': jax.random.uniform(ks[7], (OUT_C,), jnp.float32, -s_in2, s_in2), 'W_gate': jax.random.uniform(ks[8], (3 * OUT_C, 3), jnp.float32, -s_g, s_g), 'b_gate': jax.random.uniform(ks[9], (3,), jnp.float32, -s_g, s_g)}
    _L3_gnn_all = _L3_gnn_setup()
    _L3_gnn_in = {k: v for k, v in _L3_gnn_all.items() if k in ('W_src', 'b_src', 'W_dst', 'b_dst', 'W_edge', 'b_edge', 'W_gate', 'b_gate')}
    del _L3_gnn_all
    return {'x': x, 'src': src, 'dst': dst, 'edge_attr_128': edge_attr_128, 'L0_gnn_w1': _L0_gnn_in['w1'], 'L0_gnn_b1': _L0_gnn_in['b1'], 'L0_gnn_w2': _L0_gnn_in['w2'], 'L0_gnn_b2': _L0_gnn_in['b2'], 'L1_gnn_Wq': _L1_gnn_in['Wq'], 'L1_gnn_bq': _L1_gnn_in['bq'], 'L1_gnn_Wk': _L1_gnn_in['Wk'], 'L1_gnn_bk': _L1_gnn_in['bk'], 'L1_gnn_Wv': _L1_gnn_in['Wv'], 'L1_gnn_bv': _L1_gnn_in['bv'], 'L1_gnn_We': _L1_gnn_in['We'], 'L1_gnn_Wskip': _L1_gnn_in['Wskip'], 'L1_gnn_bskip': _L1_gnn_in['bskip'], 'L1_gnn_Wbeta': _L1_gnn_in['Wbeta'], 'L1_gnn_ln_gamma': _L1_gnn_in['ln_gamma'], 'L1_gnn_ln_beta': _L1_gnn_in['ln_beta'], 'L2_gnn_W_neigh1': _L2_gnn_in['W_neigh1'], 'L2_gnn_b_neigh1': _L2_gnn_in['b_neigh1'], 'L2_gnn_W_self1': _L2_gnn_in['W_self1'], 'L2_gnn_b_self1': _L2_gnn_in['b_self1'], 'L2_gnn_W_neigh2': _L2_gnn_in['W_neigh2'], 'L2_gnn_b_neigh2': _L2_gnn_in['b_neigh2'], 'L2_gnn_W_self2': _L2_gnn_in['W_self2'], 'L2_gnn_b_self2': _L2_gnn_in['b_self2'], 'L3_gnn_W_src': _L3_gnn_in['W_src'], 'L3_gnn_b_src': _L3_gnn_in['b_src'], 'L3_gnn_W_dst': _L3_gnn_in['W_dst'], 'L3_gnn_b_dst': _L3_gnn_in['b_dst'], 'L3_gnn_W_edge': _L3_gnn_in['W_edge'], 'L3_gnn_b_edge': _L3_gnn_in['b_edge'], 'L3_gnn_W_gate': _L3_gnn_in['W_gate'], 'L3_gnn_b_gate': _L3_gnn_in['b_gate']}

def reference(x, src, dst, edge_attr_128, L0_gnn_w1, L0_gnn_b1, L0_gnn_w2, L0_gnn_b2, L1_gnn_Wq, L1_gnn_bq, L1_gnn_Wk, L1_gnn_bk, L1_gnn_Wv, L1_gnn_bv, L1_gnn_We, L1_gnn_Wskip, L1_gnn_bskip, L1_gnn_Wbeta, L1_gnn_ln_gamma, L1_gnn_ln_beta, L2_gnn_W_neigh1, L2_gnn_b_neigh1, L2_gnn_W_self1, L2_gnn_b_self1, L2_gnn_W_neigh2, L2_gnn_b_neigh2, L2_gnn_W_self2, L2_gnn_b_self2, L3_gnn_W_src, L3_gnn_b_src, L3_gnn_W_dst, L3_gnn_b_dst, L3_gnn_W_edge, L3_gnn_b_edge, L3_gnn_W_gate, L3_gnn_b_gate):
    import jax
    import jax.numpy as jnp

    def _L0_gnn_ref(x, edge_index, w1, b1, w2, b2):
        import jax, jax.numpy as jnp
        import numpy as np
        N_NODES = 6250
        N_EDGES = 100000
        D = 128
        K = 2
        ALPHA = 0.5

        def _appnp(x, edge_index):
            n = x.shape[0]
            loops = jnp.arange(n, dtype=edge_index.dtype)
            src = jnp.concatenate([edge_index[0], loops])
            dst = jnp.concatenate([edge_index[1], loops])
            ew = jnp.ones_like(src, dtype=x.dtype)
            deg = jax.ops.segment_sum(ew, dst, num_segments=n)
            dinv = jnp.where(deg > 0, jax.lax.rsqrt(deg), 0.0)
            norm = dinv[src] * ew * dinv[dst]
            h = x
            for _ in range(K):
                msg = norm[:, None] * x[src]
                agg = jax.ops.segment_sum(msg, dst, num_segments=n)
                x = (1.0 - ALPHA) * agg + ALPHA * h
            return x
        x = jax.nn.relu(_appnp(x, edge_index))
        x = x @ w1.T + b1
        x = x @ w2.T + b2
        return x

    def _L1_gnn_ref(edge_state, lg_edge_index, angle_emb, Wq, bq, Wk, bk, Wv, bv, We, Wskip, bskip, Wbeta, ln_gamma, ln_beta):
        import jax, jax.numpy as jnp
        import numpy as np
        HIDDEN = 128
        HEADS = 8
        HEAD_DIM = HIDDEN // HEADS
        N_NODES = 3125
        N_EDGES = 31250
        N = edge_state.shape[0]
        H, D = (HEADS, HEAD_DIM)
        src = lg_edge_index[0]
        dst = lg_edge_index[1]
        q = (edge_state @ Wq + bq).reshape(N, H, D)
        k = (edge_state @ Wk + bk).reshape(N, H, D)
        v = (edge_state @ Wv + bv).reshape(N, H, D)
        e = (angle_emb @ We).reshape(-1, H, D)
        k_e = k[src] + e
        v_e = v[src] + e
        alpha = jnp.einsum('ehd,ehd->eh', q[dst], k_e) / jnp.sqrt(jnp.float32(D))
        m = jax.ops.segment_max(alpha, dst, num_segments=N)
        a = jnp.exp(alpha - m[dst])
        z = jax.ops.segment_sum(a, dst, num_segments=N)
        attn = a / z[dst]
        out = jax.ops.segment_sum(attn[:, :, None] * v_e, dst, num_segments=N)
        out = out.reshape(N, H * D)
        x_r = edge_state @ Wskip + bskip
        beta = jax.nn.sigmoid(jnp.concatenate([out, x_r, out - x_r], axis=-1) @ Wbeta)
        out = beta * x_r + (1.0 - beta) * out
        mu = jnp.mean(out, axis=-1, keepdims=True)
        var = jnp.mean(jnp.square(out - mu), axis=-1, keepdims=True)
        out = (out - mu) / jnp.sqrt(var + 1e-05) * ln_gamma + ln_beta
        return edge_state + jax.nn.relu(out)

    def _L2_gnn_ref(x, edge_index, W_neigh1, b_neigh1, W_self1, b_self1, W_neigh2, b_neigh2, W_self2, b_self2):
        import jax, jax.numpy as jnp
        import numpy as np
        N = 6250
        E = 100000
        D_IN = 128
        D_H = 128
        D_OUT = 128
        src, dst = (edge_index[0], edge_index[1])
        n = x.shape[0]
        deg = jax.ops.segment_sum(jnp.ones(src.shape[0], x.dtype), dst, num_segments=n)
        inv_deg = 1.0 / jnp.maximum(deg, 1.0)

        def agg(h):
            return jax.ops.segment_sum(h[src], dst, num_segments=n) * inv_deg[:, None]
        h1 = agg(x) @ W_neigh1.T + b_neigh1 + x @ W_self1.T + b_self1
        h1 = jax.nn.relu(h1)
        h2 = agg(h1) @ W_neigh2.T + b_neigh2 + h1 @ W_self2.T + b_self2
        return h2

    def _L3_gnn_ref(x, edge_index, W_src, b_src, W_dst, b_dst, W_edge, b_edge, W_gate, b_gate):
        import jax, jax.numpy as jnp
        import numpy as np
        IN_C = 128
        OUT_C = 128
        N_NODES = 3125
        N_EDGES = 50000
        row, col = (edge_index[0], edge_index[1])
        xr = x[row]
        xc = x[col]
        x_src = xr @ W_src + b_src
        x_dst = xc @ W_dst + b_dst
        x_edge = jnp.concatenate([xr, xc], axis=-1) @ W_edge + b_edge
        gate_in = jnp.concatenate([x_src, x_dst, x_edge], axis=-1)
        gates = jax.nn.softmax(gate_in @ W_gate + b_gate, axis=-1)
        out = gates[:, 0:1] * x_src + gates[:, 1:2] * x_dst + gates[:, 2:3] * x_edge
        return jax.ops.segment_sum(out, col, num_segments=x.shape[0])
    edge_index = jnp.stack([src, dst])
    h = jnp.maximum(_layernorm(x, axis=-1), 0.0)
    x = x + _L0_gnn_ref(h, edge_index, L0_gnn_w1, L0_gnn_b1, L0_gnn_w2, L0_gnn_b2)
    h = jnp.maximum(_layernorm(x, axis=-1), 0.0)
    x = x + _L1_gnn_ref(h, edge_index, edge_attr_128, L1_gnn_Wq, L1_gnn_bq, L1_gnn_Wk, L1_gnn_bk, L1_gnn_Wv, L1_gnn_bv, L1_gnn_We, L1_gnn_Wskip, L1_gnn_bskip, L1_gnn_Wbeta, L1_gnn_ln_gamma, L1_gnn_ln_beta)
    h = jnp.maximum(_layernorm(x, axis=-1), 0.0)
    x = x + _L2_gnn_ref(h, edge_index, L2_gnn_W_neigh1, L2_gnn_b_neigh1, L2_gnn_W_self1, L2_gnn_b_self1, L2_gnn_W_neigh2, L2_gnn_b_neigh2, L2_gnn_W_self2, L2_gnn_b_self2)
    h = jnp.maximum(_layernorm(x, axis=-1), 0.0)
    x = x + _L3_gnn_ref(h, edge_index, L3_gnn_W_src, L3_gnn_b_src, L3_gnn_W_dst, L3_gnn_b_dst, L3_gnn_W_edge, L3_gnn_b_edge, L3_gnn_W_gate, L3_gnn_b_gate)
    return x

_drawn_inputs = setup_inputs


def setup_inputs(seed=0):
    import zlib

    import numpy as np

    out = dict(_drawn_inputs(seed))
    spreads = {'L0_gnn_b1': (0.0, 0.1),
     'L0_gnn_b2': (0.0, 0.1),
     'L1_gnn_bq': (0.0, 0.611),
     'L1_gnn_bk': (0.0, 0.8),
     'L1_gnn_bv': (0.0, 0.1),
     'L1_gnn_bskip': (0.0, 0.1),
     'L1_gnn_ln_gamma': (1.0, 0.2),
     'L1_gnn_ln_beta': (0.0, 0.1)}
    factors = {'L2_gnn_b_neigh1': 4.223, 'L2_gnn_b_self1': 3.78, 'L3_gnn_b_gate': 3.281}
    for name, (base, spread) in spreads.items():
        noise = np.random.default_rng([zlib.crc32(name.encode()), seed]).standard_normal(out[name].shape)
        drawn = base * np.exp(spread * noise) if base else spread * noise
        out[name] = jnp.asarray(drawn.astype(out[name].dtype))
    for name, factor in factors.items():
        out[name] = (out[name] * factor).astype(out[name].dtype)
    return out
```

```python
import numpy as np
import concourse.bass as bass
from concourse import mybir
from contextlib import ExitStack, contextmanager

P = 128
NODES, EDGES, D = 6250, 100000, 128
HEADS = 8
HEAD_DIM = D // HEADS
BLOCKS = -(-NODES // P)
TAIL = NODES - (BLOCKS - 1) * P
TILES = -(-EDGES // P)
STEPS_MAX = TILES + BLOCKS - 1
U = 4
PARTS = 4
TURN = PARTS * U
TURNS = -(-STEPS_MAX // TURN)
STEPS = TURNS * TURN
ALL_PARTS = TURNS * PARTS
CHUNKS = -(-STEPS // P)
STEP_PAD = CHUNKS * P
GROUP = 7
GROUPS = BLOCKS // GROUP
assert GROUPS * GROUP == BLOCKS
HIST_TILES = 8
HIST_TURNS = TILES // (2 * HIST_TILES) + 1
HIST_PAD = HIST_TURNS * 2 * HIST_TILES
KV = 2 * D
GATE_ROW = 2 * D + 4
ATT_W = D + HEADS
GATE_W = D + 4
RUNS = P // HEADS
RUN = STEPS // RUNS * P
W_BLOCKS = -(-STEPS * HEADS // D)
BIG = 1.0e37
EPS = 1e-5
BANK = 512
TURNED = 4
LIN_TABLES = (16, 32, 80, 96)
KV_TABLE, GATE_TABLE = 64, 144
WEIGHTS = """L0_w1 L0_w2t L1_Wq L1_Wk L1_Wv L1_We L1_Wskip L2_Wn1t L2_Ws1t L2_Wn2t L2_Ws2t
    L3_Wsrc L3_Wedge_src L3_Wdst L3_Wedge_dst""".split()
WEIGHTS_ONCE = "L3_Wsrc_t L3_Wedge_src_t L3_Wdst_t L3_Wedge_dst_t".split()
BIASES = """L0_b2 L1_bq L1_bk L1_bv L1_bskip L1_gamma L1_beta L1_Wbeta_out L1_Wbeta_skip
    L2_bn1 L2_bn2 L3_b_src L3_b_dst L3_b_edge""".split()
BIASES_ONCE = "L1_Wbeta_diff L2_bs1 L2_bs2".split()


def wait(engine, sem, value):
    if not (isinstance(value, int) and value <= 0):
        engine.wait_ge(sem, value)


def edge_loop(engine, stages):
    for r in range(PARTS):
        for lag, step in stages:
            if r >= lag:
                step((r - lag) // PARTS, (r - lag) % PARTS)
    with engine.Fori(1, TURNS) as i:
        for r in range(PARTS):
            for lag, step in stages:
                back = (r - lag) // PARTS
                step(i + back if back else i, (r - lag) % PARTS)
    for late in range(max(lag for lag, _ in stages)):
        for lag, step in stages:
            if late < lag:
                step(TURNS + (late - lag) // PARTS, (late - lag) % PARTS)


class Chain:

    def __init__(self, engine, sem):
        self.engine, self.sem, self.count, self.turn = engine, sem, 0, None

    def after(self, instruction):
        instruction.then_inc(self.sem, 1)
        self.count += 1
        self.engine.wait_ge(self.sem, self.count if self.turn is None else self.turn + self.count)

    @contextmanager
    def loop(self, turns, per_turn):
        base = self.count
        with self.engine.Fori(0, turns) as i:
            self.turn = i * per_turn
            yield i
            assert self.count - base == per_turn, (self.count - base, per_turn)
        self.turn = None
        self.count = base + turns * per_turn


def program(nc, a, out):
    F32, I32, BF16 = mybir.dt.float32, mybir.dt.int32, mybir.dt.bfloat16
    ALU, ACT, AX = mybir.AluOpType, mybir.ActivationFunctionType, mybir.AxisListType
    PE, DVE, SP = mybir.EngineType.PE, mybir.EngineType.DVE, mybir.EngineType.SP
    ds = bass.ds

    with ExitStack() as ctx:
        def sb(name, shape, dtype=F32):
            return ctx.enter_context(nc.sbuf_tensor(name, shape, dtype))

        def scratch(name, shape, dtype=F32):
            return nc.dram_tensor(name, shape, dtype).ap()

        def node_rows(table):
            return table.rearrange("(b p) f -> p b f", p=P)

        def part(buffer, at, shape, dtype=F32):
            size = int(np.prod(shape)) * (2 if dtype == BF16 else 4) // 4
            v = buffer[:, at:at + size]
            if dtype != F32:
                v = v.bitcast(dtype)
            if len(shape) > 1:
                names = "abc"[:len(shape)]
                v = v.rearrange(f"p ({' '.join(names)}) -> p {' '.join(names)}", **dict(zip(names[1:], shape[1:])))
            return v

        tab_lin = [scratch(f"tab_lin{j}", (BLOCKS * P, D)) for j in range(4)]
        tab_kv = scratch("tab_kv", (BLOCKS * P, KV))
        tab_gate = scratch("tab_gate", (BLOCKS * P, GATE_ROW))
        d_block = scratch("d_block", (STEP_PAD,), I32)
        d_row0 = scratch("d_row0", (STEP_PAD,), I32)
        d_reset = scratch("d_reset", (STEP_PAD, P))
        d_value = scratch("d_value", (P, STEPS, D))

        x_flat, h_flat = sb("x", [P, BLOCKS * D]), sb("h", [P, BLOCKS * GATE_W])
        t_flat, w_flat = sb("t", [P, max(W_BLOCKS * D, BLOCKS * ATT_W)]), sb("w", [P, W_BLOCKS * D])
        acc_flat = sb("acc", [P, BLOCKS * ATT_W])

        def by_block(flat, n=BLOCKS, width=D):
            return flat[:, 0:n * width].rearrange("p (b f) -> p b f", f=width)

        x, h, t, w, acc = (by_block(v) for v in (x_flat, h_flat, t_flat, w_flat, acc_flat))
        stat = sb("stat", [P, 8, BLOCKS])
        dinv, half_dinv, inv_deg = (sb(n, [P, BLOCKS]) for n in ("dinv", "half_dinv", "inv_deg"))
        logits_src = sb("logits_src", [P, BLOCKS, 4])
        logits_dst = sb("logits_dst", [P, BLOCKS, 4])
        rel_col = sb("rel_col", [P, STEP_PAD])
        src_col = sb("src_col", [P, STEP_PAD], I32)
        step_rows = sb("step_rows", [2, STEP_PAD], I32)
        block_row, row0_row = step_rows[0:1, :], step_rows[1:2, :]
        iota = sb("iota", [P, P])
        iota_bf = sb("iota_bf", [P, P], BF16)
        ident = sb("ident", [P, P])
        weights = sb("weights", [P, len(WEIGHTS), D])
        biases = sb("biases", [P, len(BIASES), D])
        bias_cols = sb("bias_cols", [P, 4])
        w_gate = sb("w_gate", [P, 3, 3])
        b_gate = sb("b_gate", [P, 3])
        w_logit = sb("w_logit", [P, 8])
        b_logit = sb("b_logit", [P, 8])
        idx = sb("idx", [P, PARTS, U], I32)
        rows_flat = sb("rows", [P, TURN * GATE_ROW])
        rows = rows_flat[:].rearrange("p (q f) -> p q f", f=GATE_ROW)
        hot = sb("hot", [P, TURN, P])
        hot_t = sb("hot_t", [P, 2, U * P])
        edge_flat = sb("edge", [P, TURN * GATE_W])
        attr = part(edge_flat, 0, (TURN, D))
        attr_t = sb("attr_t", [P, 2, U * D])
        value = sb("value", [P, 2 * U, D])
        small = sb("small", [P, 2, 64])
        stage = [part(rows_flat, k * GROUP * D, (GROUP, D)) for k in range(2)]
        stage_t = [part(rows_flat, (2 + k) * GROUP * D, (GROUP, D)) for k in range(2)]
        stage_o = part(edge_flat, 0, (GROUP, D))
        msg_att = part(rows_flat, 0, (TURN, ATT_W))
        msg_gate = part(edge_flat, 0, (TURN, GATE_W))
        scaled = value[:, 0:U, :]
        turned = part(rows_flat, 0, (TURNED, RUNS, HEADS))
        setup, blk = part(t_flat, 0, (6, TILES)), part(t_flat, 6 * TILES, (2, TILES), I32)
        tile_ends = part(h_flat, 0, (2, TILES), I32)
        dst_cols = part(h_flat, 2 * TILES, (HIST_PAD,), I32)
        lohi = part(h_flat, 2 * TILES + HIST_PAD, (2, HIST_PAD))
        lohi_i = part(h_flat, 2 * TILES + 3 * HIST_PAD, (2, HIST_PAD), I32)
        hot_lo = [part(rows_flat, k * HIST_TILES * P // 2, (HIST_TILES, P), BF16) for k in range(2)]
        hot_hi = [part(rows_flat, HIST_TILES * P + k * HIST_TILES * 32, (HIST_TILES, 64), BF16)[:, :, 0:BLOCKS] for k in range(2)]
        bias_wide = part(edge_flat, 0, (4, D))
        weights_once = part(edge_flat, 4 * D, (len(WEIGHTS_ONCE), D))
        biases_once = part(edge_flat, (4 + len(WEIGHTS_ONCE)) * D, (len(BIASES_ONCE), D))
        step_no = sb("step_no", [P, CHUNKS])
        step_f = sb("step_f", [P, 5, CHUNKS])
        before = sb("before", [P, CHUNKS], I32)
        step_i = sb("step_i", [P, 3, CHUNKS], I32)
        edge_i = part(w_flat, 0, (2 * CHUNKS, P), I32)
        edge_f = [part(acc_flat, k * CHUNKS * P, (CHUNKS, P)) for k in range(4)]
        REL, SRC, RESET, LAST = range(4)
        score = w_flat[:, 0:STEPS * HEADS]
        by_run = score.rearrange("p (j q h) -> p q j h", j=RUNS, h=HEADS)
        run_row = attr_t[0:1, :, :].rearrange("o a b -> o (a b)")[:, 0:6 * P].rearrange("o (m k) -> o m k", k=P)
        run_col = sb("run_col", [P, 8])

        ps = ctx.enter_context(nc.psum_tensor("ps", [P, 8 * BANK], F32))

        def banks(first, n=1):
            return ps[:, first * BANK:(first + n) * BANK]

        block = ctx.enter_context(nc.Block())
        sems = {}

        def sem(name):
            if name not in sems:
                sems[name] = ctx.enter_context(nc.semaphore(name))
            return sems[name]

        rows_in = [sem(f"rows_in{r}") for r in range(PARTS)]
        attr_in = [sem(f"attr_in{r}") for r in range(PARTS)]
        value_out = [sem(f"value_out{r}") for r in range(2)]
        value_in = [sem(f"value_in{r}") for r in range(PARTS)]

        def by_node(v, width=D):
            return v.unsqueeze(2).broadcast_to((P, BLOCKS, width))

        def bias(name, n=BLOCKS):
            return biases[:, BIASES.index(name), :].unsqueeze(1).broadcast_to((P, n, D))

        def weight(name):
            return weights_once[:, WEIGHTS_ONCE.index(name), :] if name in WEIGHTS_ONCE else weights[:, WEIGHTS.index(name), :]

        def registers(engine_type, row, i, r, top):
            _, values = nc.values_load_multi_w_load_instructions(
                row[0:1, ds((i * PARTS + r) * U, U)], engines=[engine_type], min_val=0, max_val=top,
                skip_runtime_bounds_check_because="the tables are clamped when they are made")
            return values


        def step_idx(act, k):
            def step(i, r):
                wait(act, rows_in[r], 16 * U * (k * TURNS + i))
                act.sem_inc(sem("act_turn"), 1)
                nc.scalar.activation(idx[:, r, :], src_col[:, ds((i * PARTS + r) * U, U)],
                                     ACT.Copy).then_inc(sem("idx_ready"), 1)
            return step

        def step_gather(pool, k, table, width, free):
            def step(i, r):
                pool.wait_ge(sem("idx_ready"), k * ALL_PARTS + i * PARTS + r + 1)
                free(i, r)
                pool.sem_inc(sem("pool_turn"), 1)
                for u in range(U):
                    q = r * U + u
                    pool.indirect_dma_start(rows[:, q, 0:width], None, table,
                                            bass.IndirectOffsetOnAxis(idx[:, r, u:u + 1], 0)).then_inc(rows_in[r], 16)
            return step

        def step_hot(free=lambda i, r: None):
            def step(i, r):
                free(i, r)
                nc.vector.tensor_tensor(hot[:, r * U:(r + 1) * U, :], iota[:].unsqueeze(1).broadcast_to((P, U, P)),
                                        rel_col[:, ds((i * PARTS + r) * U, U)].unsqueeze(2).broadcast_to((P, U, P)),
                                        ALU.is_equal).then_inc(sem("hot_ready"), 1)
            return step

        class Sums:
            def __init__(self, order, hot_loops, width, first, ring, into=(acc_flat,)):
                self.width, self.first, self.ring = width, first, ring
                self.into = [by_block(flat, BLOCKS, width) for flat in into]
                self.share = 4 if 4 * width <= BANK else 2
                self.hot0 = hot_loops * ALL_PARTS
                self.done0 = order * STEPS
                self.added0 = order * (STEPS + TURN)

            def place(self, r, u):
                at = (self.first + (r % self.ring) * (U // self.share) + u // self.share) * BANK \
                    + (u % self.share) * BANK // self.share
                return ps[:, at:at + self.width]

            def start(self, dve):
                dve.sem_inc(sem("win_added"), TURN)

            def free(self, engine, i, r, back):
                engine.wait_ge(sem("win_added"), self.added0 + U * (i * PARTS + r) + U * (PARTS - back + 1))

            def step_pe(self, pe, message, arrived):
                def step(i, r):
                    pe.wait_ge(sem("hot_ready"), self.hot0 + i * PARTS + r + 1)
                    self.free(pe, i, r, self.ring)
                    arrived(i, r)
                    pe.sem_inc(sem("pe_turn"), 1)
                    for u in range(U):
                        nc.tensor.matmul(self.place(r, u), hot[:, r * U + u, :], message(r, u),
                                         start=True, stop=True).then_inc(sem("win_done"), 1)
                return step

            def step_add(self, dve):
                m = len(self.into)

                def step(i, r):
                    n = U * (i * PARTS + r)
                    blocks = registers(DVE, block_row, i, r, BLOCKS - 1)
                    dve.wait_ge(sem("win_done"), self.done0 + n + U)
                    for u in range(U):
                        if u % m == 0:
                            dve.wait_ge(sem("win_added"), self.added0 + TURN + n + u)
                        nodes = self.into[u % m][:, ds(blocks[u], 1), :].rearrange("p b f -> p (b f)")
                        nc.vector.tensor_tensor(nodes, nodes, self.place(r, u), ALU.add).then_inc(sem("win_added"), 1)
                return step

            def end(self, dve):
                dve.wait_ge(sem("win_added"), self.added0 + TURN + STEPS)

        LIN_PASS, ATT_PASS, GATE_PASS = (0, 1, 3, 4), 2, 5
        linear = [Sums(order, loops, D, 0, PARTS) for order, loops in ((0, 0), (1, 1), (3, 4), (4, 5))]
        att_sums = Sums(2, 3, ATT_W, 0, PARTS, (acc_flat, t_flat))
        gate_sums = Sums(5, 6, GATE_W, 4, 2, (acc_flat, h_flat))
        ATT_HOT0, GATE_HOT0 = 2 * ALL_PARTS, 6 * ALL_PARTS

        def lin_act(act, j):
            edge_loop(act, [(0, step_idx(act, LIN_PASS[j]))])

        def lin_pool(pool, j):
            pool.wait_ge(sem("table_out"), LIN_TABLES[j])
            edge_loop(pool, [(0, step_gather(pool, LIN_PASS[j], tab_lin[j], D,
                                             lambda i, r: linear[j].free(pool, i, r, PARTS)))])

        def lin_pe(pe, j):
            edge_loop(pe, [(0, linear[j].step_pe(
                pe, lambda r, u: rows[:, r * U + u, 0:D],
                lambda i, r: pe.wait_ge(rows_in[r], 16 * U * (LIN_PASS[j] * TURNS + i + 1))))])

        def lin_dve(dve, chain, j):
            chain.after(nc.vector.memset(acc_flat[:, 0:BLOCKS * D], 0.0))
            linear[j].start(dve)
            edge_loop(dve, [(0, step_hot()), (1, linear[j].step_add(dve))])
            linear[j].end(dve)


        class Products:
            all = []

            def __init__(self, event, sources, outputs, late=False):
                self.late, self.late0 = late, sum(GROUPS for p in self.all if p.late)
                self.event, self.sources, self.outputs = event, sources, outputs
                self.src0 = sum(GROUPS * len(p.sources) for p in self.all)
                self.out0 = sum(GROUPS * len(p.outputs) for p in self.all)
                self.used0 = sum((GROUPS + 1) * len(p.outputs) for p in self.all)
                self.all.append(self)

            def place(self, o):
                return banks(4 + 2 * (o % 2), 2)

            def act(self, act):
                act.wait_ge(sem(self.event), 1)
                m = len(self.sources)
                with act.Fori(0, GROUPS) as g:
                    for k, source in enumerate(self.sources):
                        nc.scalar.activation(stage[k], source[:, ds(g * GROUP, GROUP), :], ACT.Copy).then_inc(sem("g_staged"), 1)
                    for k in range(m):
                        act.wait_ge(sem("g_t"), self.src0 + g * m + k + 1)
                        nc.scalar.activation(stage_t[k], banks(2 * k, 2)[:, 0:GROUP * P].rearrange("p (b f) -> p b f", f=P),
                                             ACT.Copy).then_inc(sem("g_t_copied"), 1)

            def pe(self, pe):
                pe.wait_ge(sem(self.event), 1)
                m, n = len(self.sources), len(self.outputs)
                with pe.Fori(0, GROUPS) as g:
                    for k in range(m):
                        pe.wait_ge(sem("g_staged"), self.src0 + g * m + k + 1)
                        for j in range(GROUP):
                            last = nc.tensor.transpose(banks(2 * k, 2)[:, j * P:(j + 1) * P], stage[k][:, j, :], ident[:])
                        last.then_inc(sem("g_t"), 1)
                    pe.wait_ge(sem("g_t_copied"), self.src0 + g * m + m)
                    for o, (mats, columns, _) in enumerate(self.outputs):
                        before = o - 2 if o >= 2 else max(b for b in range(n) if b % 2 == o % 2) - n
                        pe.wait_ge(sem("g_used"), self.used0 + g * n + n + before + 1)
                        pe.sem_inc(sem("pe_turn"), 1)
                        for j in range(GROUP):
                            at = self.place(o)[:, j * P:j * P + columns]
                            for k in range(m):
                                last = nc.tensor.matmul(at, stage_t[k][:, j, :], mats[k], start=k == 0, stop=k == m - 1)
                        last.then_inc(sem("g_out"), 1)

            def dve(self, dve):
                n = len(self.outputs)
                dve.sem_inc(sem("g_used"), n)
                dve.sem_inc(sem(self.event), 1)
                with dve.Fori(0, GROUPS) as g:
                    for o, (_, columns, take) in enumerate(self.outputs):
                        dve.wait_ge(sem("g_out"), self.out0 + g * n + o + 1)
                        dve.sem_inc(sem("dve_turn"), 1)
                        src = self.place(o)[:, 0:GROUP * P].rearrange("p (b f) -> p b f", f=P)[:, :, 0:columns]

                        def taken(ins, o=o):
                            ins.then_inc(sem("g_used"), 1)
                            dve.wait_ge(sem("g_used"), self.used0 + n + g * n + o + 1)

                        def late(ins):
                            ins.then_inc(sem("late"), 1)
                            dve.wait_ge(sem("late"), self.late0 + g + 1)
                        take(g, src, taken, late)

        def with_bias(target, name, relu=False):
            def take(g, src, taken, late):
                rows_g = target[:, ds(g * GROUP, GROUP), :]
                if relu:
                    taken(nc.vector.tensor_tensor(stage_o, src, bias(name, GROUP), ALU.add))
                    late(nc.vector.tensor_scalar(rows_g, stage_o, 0.0, None, ALU.max))
                else:
                    taken(nc.vector.tensor_tensor(rows_g, src, bias(name, GROUP), ALU.add))
            return take

        def into_x(name):
            def take(g, src, taken, late):
                rows_g = x[:, ds(g * GROUP, GROUP), :]
                taken(nc.vector.tensor_tensor(stage_o, src, bias(name, GROUP), ALU.add))
                late(nc.vector.tensor_tensor(rows_g, rows_g, stage_o, ALU.add))
            return take

        def take_logits(g, src, taken, late):
            wide = b_logit[:].unsqueeze(1).broadcast_to((P, GROUP, 8))
            nc.vector.tensor_tensor(logits_src[:, ds(g * GROUP, GROUP), :], src[:, :, 0:4], wide[:, :, 0:4], ALU.add)
            taken(nc.vector.tensor_tensor(logits_dst[:, ds(g * GROUP, GROUP), :], src[:, :, 4:8], wide[:, :, 4:8], ALU.add))

        p_l0 = Products("l0_ready", [w], [([weight("L0_w1")], D, into_x("L0_b2"))], True)
        p_qkv = Products("qkv_ready", [h], [([weight("L1_Wq")], D, with_bias(t, "L1_bq")),
                                            ([weight("L1_Wk")], D, with_bias(acc, "L1_bk")),
                                            ([weight("L1_Wv")], D, with_bias(w, "L1_bv"))])
        p_skip = Products("skip_ready", [h], [([weight("L1_Wskip")], D, with_bias(t, "L1_bskip"))])
        p_sage1 = Products("sage1_ready", [w, h], [([weight("L2_Wn1t"), weight("L2_Ws1t")], D, with_bias(t, "L2_bn1", True))], True)
        p_sage2 = Products("sage2_ready", [w, t], [([weight("L2_Wn2t"), weight("L2_Ws2t")], D, into_x("L2_bn2"))], True)
        p_gate = Products("gate_ready", [h], [([weight("L3_Wsrc")], D, with_bias(acc, "L3_b_src")),
                                              ([weight("L3_Wdst")], D, with_bias(t, "L3_b_dst")),
                                              ([weight("L3_Wedge_dst")], D, with_bias(w, "L3_b_edge")),
                                              ([w_logit[:]], 8, take_logits),
                                              ([weight("L3_Wedge_src")], D, lambda g, src, taken, late: taken(
                                                  nc.vector.tensor_copy(h[:, ds(g * GROUP, GROUP), :], src)))])


        def norm_act(act, n):
            act.wait_ge(sem("ln_centred"), n + 1)
            nc.scalar.activation(acc, w, ACT.Square).then_inc(sem("sq_ready"), 1)

        def root_act(act, m):
            act.wait_ge(sem("var_ready"), m + 1)
            nc.scalar.activation(stat[:, 4, :], stat[:, 3, :], ACT.Sqrt).then_inc(sem("root_ready"), 1)

        def rsqrt_dve(dve, chain, m, result):
            dve.wait_ge(sem("root_ready"), m + 1)
            chain.after(nc.vector.reciprocal(stat[:, 5, :], stat[:, 4, :]))
            chain.after(nc.vector.tensor_tensor(stat[:, 6, :], stat[:, 5, :], stat[:, 5, :], ALU.mult))
            chain.after(nc.vector.tensor_tensor(stat[:, 6, :], stat[:, 6, :], stat[:, 3, :], ALU.mult))
            chain.after(nc.vector.tensor_scalar(stat[:, 6, :], stat[:, 6, :], -0.5, 1.5, ALU.mult, ALU.add))
            chain.after(nc.vector.tensor_tensor(result, stat[:, 5, :], stat[:, 6, :], ALU.mult))

        def norm_dve(dve, chain, n, m, source):
            chain.after(nc.vector.tensor_reduce(stat[:, 0, :], source, AX.X, ALU.add))
            chain.after(nc.vector.tensor_scalar(stat[:, 1, :], stat[:, 0, :], 1.0 / D, None, ALU.mult))
            nc.vector.tensor_tensor(w, source, by_node(stat[:, 1, :]), ALU.subtract).then_inc(sem("ln_centred"), 1)
            dve.wait_ge(sem("sq_ready"), n + 1)
            chain.after(nc.vector.tensor_reduce(stat[:, 2, :], acc, AX.X, ALU.add))
            nc.vector.tensor_scalar(stat[:, 3, :], stat[:, 2, :], 1.0 / D, EPS, ALU.mult, ALU.add).then_inc(sem("var_ready"), 1)
            rsqrt_dve(dve, chain, m, stat[:, 7, :])

        def norm_relu_dve(dve, chain, n, m):
            norm_dve(dve, chain, n, m, x)
            chain.after(nc.vector.scalar_tensor_tensor(h, w, 0.0, by_node(stat[:, 7, :]), ALU.max, ALU.mult))

        ATT_TURN0 = ATT_PASS * TURNS
        RING2 = 2

        def att_sp(sp):
            def load(i, r):
                n = i * PARTS + r
                row0 = registers(SP, row0_row, i, r, (TILES - 1) * P)
                wait(sp, sem("att_turned"), n - PARTS + 1)
                for u in range(U):
                    q = r * U + u
                    sp.dma_start(attr[:, q, :], a["attr"][ds(row0[u], P), :]).then_inc(attr_in[r], 16)

            def store(i, r):
                n = i * PARTS + r
                sp.wait_ge(sem("kv_done"), n + 1)
                sp.dma_start(d_value[:, ds(n * U, U), :], value[:, r % RING2 * U:(r % RING2 + 1) * U, :]).then_inc(value_out[r % RING2], 16)
            edge_loop(sp, [(0, load), (3, store)])

        def att_pool(pool):
            pool.wait_ge(sem("table_out"), KV_TABLE)
            edge_loop(pool, [(0, step_gather(pool, ATT_PASS, tab_kv, KV, lambda i, r: wait(
                pool, sem("kv_done"), i * PARTS + r - PARTS + 1)))])

        def att_act(act):
            def copy(i, r):
                n = i * PARTS + r
                act.wait_ge(sem("att_turned"), n + 1)
                wait(act, sem("eq_done"), n - RING2 + 1)
                nc.scalar.activation(attr_t[:, r % RING2], banks(0), ACT.Copy).then_inc(sem("att_copied"), 1)
                nc.scalar.activation(hot_t[:, r % RING2], banks(1), ACT.Copy).then_inc(sem("att_copied"), 1)
            edge_loop(act, [(0, step_idx(act, ATT_PASS)), (0, copy)])

        def att_pe(pe):
            def turn(i, r):
                n = i * PARTS + r
                pe.wait_ge(attr_in[r], 16 * U * (i + 1))
                pe.wait_ge(sem("hot_ready"), ATT_HOT0 + n + 1)
                wait(pe, sem("att_copied"), 2 * n)
                for u in range(U):
                    nc.tensor.transpose(banks(0)[:, u * D:(u + 1) * D], attr[:, r * U + u, :], ident[:])
                for u in range(U):
                    last = nc.tensor.transpose(banks(1)[:, u * P:(u + 1) * P], hot[:, r * U + u, :], ident[:])
                last.then_inc(sem("att_turned"), 1)

            def products(i, r):
                n = i * PARTS + r
                blocks = registers(PE, block_row, i, r, BLOCKS - 1)
                pe.wait_ge(sem("att_copied"), 2 * n + 2)
                wait(pe, sem("kv_done"), n - RING2 + 1)
                pe.sem_inc(sem("pe_turn"), 1)
                e, q = banks(2 + 2 * (r % RING2)), banks(3 + 2 * (r % RING2))
                for u in range(U):
                    nc.tensor.matmul(e[:, u * D:(u + 1) * D], attr_t[:, r % RING2, u * D:(u + 1) * D], weight("L1_We"), start=True, stop=True)
                for u in range(U):
                    last = nc.tensor.matmul(q[:, u * D:(u + 1) * D], hot_t[:, r % RING2, u * P:(u + 1) * P],
                                            t[:, ds(blocks[u], 1), :].rearrange("p b f -> p (b f)"), start=True, stop=True)
                last.then_inc(sem("eq_done"), 1)
            edge_loop(pe, [(0, turn), (1, products)])

        def att_dve(dve):
            def scores(i, r):
                n = i * PARTS + r
                e = banks(2 + 2 * (r % RING2)).rearrange("p (u f) -> p u f", u=U)
                q = banks(3 + 2 * (r % RING2)).rearrange("p (u f) -> p u f", u=U)
                key = rows[:, r * U:(r + 1) * U, 0:D]
                values = value[:, r % RING2 * U:(r % RING2 + 1) * U, :]
                dve.wait_ge(sem("eq_done"), n + 1)
                dve.wait_ge(rows_in[r], 16 * U * (ATT_TURN0 + i + 1))
                wait(dve, value_out[r % RING2], 16 * (i * (PARTS // RING2) + r // RING2))
                nc.vector.tensor_tensor(key, e, key, ALU.add).then_inc(sem("key_step"), 1)
                nc.vector.tensor_tensor(values, e, rows[:, r * U:(r + 1) * U, D:KV], ALU.add)
                dve.wait_ge(sem("key_step"), 2 * n + 1)
                nc.vector.tensor_tensor(key, key, q, ALU.mult).then_inc(sem("key_step"), 1)
                dve.wait_ge(sem("key_step"), 2 * n + 2)
                dve.sem_inc(sem("dve_turn"), 1)
                nc.vector.tensor_reduce(score[:, ds(n * U * HEADS, U * HEADS)].rearrange("p (u h) -> p u h", h=HEADS),
                                        key.rearrange("p u (h d) -> p u h d", d=HEAD_DIM), AX.X, ALU.add).then_inc(sem("kv_done"), 1)
            edge_loop(dve, [(0, step_hot()), (2, scores)])
            dve.wait_ge(sem("kv_done"), ALL_PARTS)
            dve.sem_inc(sem("scores_ready"), 1)

        STEPS_OF_RUN = STEPS // RUNS
        TURNED_TURNS = STEPS_OF_RUN // TURNED
        resets, best = acc_flat[:, 0:RUN], t_flat[:, 0:RUN]
        turned_flat = rows_flat[:, 0:TURNED * P]
        group_ps = banks(0)[:, 0:TURNED * P]

        def max_sp(sp):
            runs = d_reset[0:STEPS, :].rearrange("(j q) e -> j (q e)", j=RUNS)
            for j in range(RUNS):
                sp.dma_start(resets[j * HEADS:(j + 1) * HEADS, :], runs[j, :].partition_broadcast(HEADS)).then_inc(sem("resets_in"), 16)

        def turn_act(act, k):
            act.wait_ge(sem("max_ready"), k + 1)
            with act.Fori(0, TURNED_TURNS) as g:
                act.wait_ge(sem("turned"), k * TURNED_TURNS + g + 1)
                act.sem_inc(sem("act_turn"), 1)
                if k == 0:
                    ins = nc.scalar.activation(turned, by_run[:, ds(g * TURNED, TURNED)], ACT.Copy)
                else:
                    ins = nc.scalar.activation(turned_flat, best[:, ds(g * TURNED * P, TURNED * P)], ACT.Copy)
                ins.then_inc(sem("turn_staged"), 1)
        def turn_pe(pe, k):
            if k == 0:
                pe.sem_inc(sem("turned"), 1)
            with pe.Fori(0, TURNED_TURNS) as g:
                pe.wait_ge(sem("turn_staged"), k * TURNED_TURNS + g + 1)
                pe.wait_ge(sem("turn_used"), k * TURNED_TURNS + g + 1)
                for m in range(TURNED):
                    last = nc.tensor.transpose(group_ps[:, m * P:(m + 1) * P], turned_flat[:, m * P:(m + 1) * P], ident[:])
                last.then_inc(sem("turned"), 1)

        def carry_pe(pe, k):
            pe.wait_ge(sem("ends_ready"), k + 1)
            for m in range(3):
                last = nc.tensor.transpose(banks(1)[0:1, m * P:(m + 1) * P], run_col[:, m:m + 1], ident[:])
            last.then_inc(sem("ends_turned"), 1)
            pe.wait_ge(sem("carry_row"), k + 1)
            nc.tensor.transpose(banks(2)[:, 0:1], run_row[0:1, 5, :], ident[0:1, 0:1]).then_inc(sem("carry_turned"), 1)

        def ends_row(m):
            return banks(1)[0:1, m * P:(m + 1) * P].rearrange("o (j h) -> o h j", h=HEADS)

        def head_run(m):
            return run_row[0:1, m, :].rearrange("o (h j) -> o h j", h=HEADS)

        def turn_dve(dve, chain, k):
            if k == 0:
                dve.sem_inc(sem("turn_used"), 1)
            dve.sem_inc(sem("max_ready"), 1)
            with dve.Fori(0, TURNED_TURNS) as g:
                dve.wait_ge(sem("turned"), k * TURNED_TURNS + g + 2)
                dve.sem_inc(sem("dve_turn"), 1)
                if k == 0:
                    nc.vector.tensor_copy(best[:, ds(g * TURNED * P, TURNED * P)], group_ps).then_inc(sem("turn_used"), 1)
                else:
                    at = by_run[:, ds(g * TURNED, TURNED)]
                    nc.vector.tensor_tensor(at, at, group_ps.rearrange("p (q j h) -> p q j h", j=RUNS, h=HEADS),
                                            ALU.subtract).then_inc(sem("turn_used"), 1)
            dve.wait_ge(sem("turn_used"), (k + 1) * TURNED_TURNS + 1)

        def max_dve(dve, chain):
            turn_dve(dve, chain, 0)
            dve.wait_ge(sem("resets_in"), 16 * RUNS)
            first, last = slice(0, 1), slice(RUN - 1, RUN)
            nc.vector.tensor_reduce(run_col[:, 1:2], resets, AX.X, ALU.min)
            nc.vector.tensor_reduce(run_col[:, 3:4], resets[:, 1:RUN], AX.X, ALU.min)
            nc.vector.tensor_copy(run_col[:, 2:3], resets[:, first])
            chain.after(nc.vector.tensor_tensor_scan(best, resets, best, -BIG, ALU.add, ALU.max))
            nc.vector.tensor_copy(run_col[:, 0:1], best[:, last]).then_inc(sem("ends_ready"), 1)
            dve.wait_ge(sem("ends_turned"), 1)
            chain.after(nc.vector.tensor_copy(head_run(0), ends_row(0)))
            chain.after(nc.vector.tensor_copy(head_run(1), ends_row(1)))
            chain.after(nc.vector.memset(head_run(1)[:, :, 0:1], -BIG))
            chain.after(nc.vector.tensor_tensor_scan(run_row[0:1, 2, :], run_row[0:1, 1, :], run_row[0:1, 0, :], -BIG, ALU.add, ALU.max))
            carry = run_row[0:1, 5, :].rearrange("o (j h) -> o h j", h=HEADS)
            chain.after(nc.vector.memset(run_row[0:1, 5, :], -BIG))
            nc.vector.tensor_copy(carry[:, :, 1:RUNS], head_run(2)[:, :, 0:RUNS - 1]).then_inc(sem("carry_row"), 1)
            dve.wait_ge(sem("carry_turned"), 1)
            chain.after(nc.vector.tensor_copy(run_col[:, 4:5], banks(2)[:, 0:1]))
            chain.after(nc.vector.tensor_tensor_scan(best, resets, best, run_col[:, 4:5], ALU.add, ALU.max))
            inner, after = best[:, 0:RUN - 1], resets[:, 1:RUN]
            chain.after(nc.vector.tensor_tensor_scan(inner[:, ::-1], after[:, ::-1], inner[:, ::-1], best[:, last], ALU.add, ALU.max))
            nc.vector.tensor_copy(run_col[:, 1:2], run_col[:, 3:4])
            nc.vector.tensor_copy(run_col[:, 0:1], best[:, first]).then_inc(sem("ends_ready"), 1)
            dve.wait_ge(sem("ends_turned"), 2)
            chain.after(nc.vector.tensor_copy(head_run(0), ends_row(0)))
            chain.after(nc.vector.tensor_copy(head_run(1), ends_row(1)))
            chain.after(nc.vector.memset(run_row[0:1, 3, :], -BIG))
            chain.after(nc.vector.tensor_copy(head_run(3)[:, :, 0:RUNS - 1], ends_row(2)[:, :, 1:RUNS]))
            chain.after(nc.vector.tensor_tensor(run_row[0:1, 1, :], run_row[0:1, 1, :], run_row[0:1, 3, :], ALU.add))
            chain.after(nc.vector.tensor_tensor_scan(run_row[0:1, 2, ::-1], run_row[0:1, 1, ::-1], run_row[0:1, 0, ::-1], -BIG, ALU.add, ALU.max))
            chain.after(nc.vector.tensor_tensor(head_run(3)[:, :, 0:RUNS - 1], head_run(3)[:, :, 0:RUNS - 1],
                                                head_run(2)[:, :, 1:RUNS], ALU.add))
            nc.vector.tensor_copy(carry, head_run(3)).then_inc(sem("carry_row"), 1)
            dve.wait_ge(sem("carry_turned"), 2)
            chain.after(nc.vector.tensor_tensor(best[:, last], best[:, last], banks(2)[:, 0:1], ALU.max))
            chain.after(nc.vector.tensor_tensor_scan(inner[:, ::-1], after[:, ::-1], inner[:, ::-1], best[:, last], ALU.add, ALU.max))
            turn_dve(dve, chain, 1)

        def sums_sp(sp):
            for r in range(RING2):
                sp.wait_ge(value_out[r], 16 * (ALL_PARTS // RING2))

            def load(i, r):
                n = i * PARTS + r
                wait(sp, sem("msg_ready"), n - PARTS + 1)
                sp.sem_inc(sem("sp_turn"), 1)
                sp.dma_start(attr[:, r * U:(r + 1) * U, :], d_value[:, ds(n * U, U), :]).then_inc(value_in[r], 16)
            edge_loop(sp, [(0, load)])

        def sums_act(act):
            act.wait_ge(sem("max_ready"), 3)
            nc.scalar.activation(score, score, ACT.Exp).then_inc(sem("exp_ready"), 1)
            act.wait_ge(sem("exp_ready"), 1)

            def weights_in(i, r):
                att_sums.free(act, i, r, PARTS)
                act.sem_inc(sem("act_turn"), 1)
                nc.scalar.activation(msg_att[:, r * U:(r + 1) * U, D:ATT_W],
                                     score[:, ds((i * PARTS + r) * U * HEADS, U * HEADS)].rearrange("p (u h) -> p u h", h=HEADS),
                                     ACT.Copy).then_inc(sem("msg_weights"), 1)
            edge_loop(act, [(0, weights_in)])

        def sums_pool(pool):
            pool.wait_ge(sem("max_ready"), 2)
            pool.memset(acc_flat[:], 0.0).then_inc(sem("sums_zeroed"), 1)
            pool.wait_ge(sem("max_ready"), 3)
            pool.memset(t_flat[:, 0:BLOCKS * ATT_W], 0.0).then_inc(sem("sums_zeroed"), 1)
            pool.wait_ge(sem("exp_ready"), 1)

            def weigh(i, r):
                n = i * PARTS + r
                pool.wait_ge(value_in[r], 16 * (i + 1))
                att_sums.free(pool, i, r, PARTS)
                pool.sem_inc(sem("pool_turn"), 1)
                wide = score[:, ds(n * U * HEADS, U * HEADS)].rearrange("p (u h) -> p u h", h=HEADS)
                pool.tensor_tensor(msg_att[:, r * U:(r + 1) * U, 0:D].rearrange("p u (h d) -> p u h d", h=HEADS),
                                   attr[:, r * U:(r + 1) * U, :].rearrange("p u (h d) -> p u h d", h=HEADS),
                                   wide.unsqueeze(3).broadcast_to((P, U, HEADS, HEAD_DIM)), ALU.mult).then_inc(sem("msg_ready"), 1)
            edge_loop(pool, [(0, weigh)])

        def sums_pe(pe):
            def arrived(i, r):
                pe.wait_ge(sem("msg_ready"), i * PARTS + r + 1)
                pe.wait_ge(sem("msg_weights"), i * PARTS + r + 1)
            edge_loop(pe, [(0, att_sums.step_pe(pe, lambda r, u: msg_att[:, r * U + u, :], arrived))])

        def sums_dve(dve, chain):
            dve.sem_inc(sem("max_ready"), 1)
            dve.wait_ge(sem("sums_zeroed"), 2)
            att_sums.start(dve)
            edge_loop(dve, [(0, step_hot()), (2, att_sums.step_add(dve))])
            att_sums.end(dve)
            chain.after(nc.vector.tensor_tensor(acc_flat[:], acc_flat[:], t_flat[:, 0:BLOCKS * ATT_W], ALU.add))

        def beta_act(act):
            act.wait_ge(sem("beta_in"), 1)
            nc.scalar.activation(stat[:, 1, :], stat[:, 0, :], ACT.Exp, scale=-1.0).then_inc(sem("beta_exp"), 1)

        def att_end_dve(dve, chain):
            sums = by_block(acc_flat, BLOCKS, ATT_W)
            rz = part(edge_flat, 0, (BLOCKS, HEADS))
            chain.after(nc.vector.tensor_scalar(rz, sums[:, :, D:ATT_W], 0.5, None, ALU.max))
            chain.after(nc.vector.reciprocal(rz, rz))
            chain.after(nc.vector.tensor_tensor(w.rearrange("p b (h d) -> p b h d", h=HEADS),
                                                sums[:, :, 0:D].rearrange("p b (h d) -> p b h d", h=HEADS),
                                                rz.unsqueeze(3).broadcast_to((P, BLOCKS, HEADS, HEAD_DIM)), ALU.mult))
            p_skip.dve(dve)
            chain.after(nc.vector.tensor_tensor(acc, w, bias("L1_Wbeta_out"), ALU.mult))
            chain.after(nc.vector.tensor_reduce(stat[:, 0, :], acc, AX.X, ALU.add))
            chain.after(nc.vector.tensor_tensor(acc, t, bias("L1_Wbeta_skip"), ALU.mult))
            chain.after(nc.vector.tensor_reduce(stat[:, 1, :], acc, AX.X, ALU.add))
            nc.vector.tensor_tensor(stat[:, 0, :], stat[:, 0, :], stat[:, 1, :], ALU.add).then_inc(sem("beta_in"), 1)
            dve.wait_ge(sem("beta_exp"), 1)
            chain.after(nc.vector.tensor_scalar(stat[:, 1, :], stat[:, 1, :], 1.0, None, ALU.add))
            chain.after(nc.vector.reciprocal(stat[:, 2, :], stat[:, 1, :]))
            chain.after(nc.vector.tensor_tensor(acc, t, w, ALU.subtract))
            chain.after(nc.vector.tensor_tensor(acc, acc, by_node(stat[:, 2, :]), ALU.mult))
            chain.after(nc.vector.tensor_tensor(w, w, acc, ALU.add))
            norm_dve(dve, chain, 2, 3, w)
            chain.after(nc.vector.tensor_tensor(w, w, by_node(stat[:, 7, :]), ALU.mult))
            chain.after(nc.vector.tensor_tensor(w, w, bias("L1_gamma"), ALU.mult))
            chain.after(nc.vector.tensor_tensor(w, w, bias("L1_beta"), ALU.add))
            chain.after(nc.vector.scalar_tensor_tensor(w, w, 0.0, h, ALU.max, ALU.add))
            chain.after(nc.vector.tensor_tensor(x, x, w, ALU.add))

        GATE_TURN0 = GATE_PASS * TURNS
        GATE1, GATE2 = D + 1, D + 2

        def gate_pool(pool):
            pool.wait_ge(sem("table_out"), GATE_TABLE)
            edge_loop(pool, [(0, step_gather(pool, GATE_PASS, tab_gate, GATE_ROW, lambda i, r: wait(
                pool, sem("gate_msg"), i * PARTS + r - PARTS + 1)))])

        def gate_act(act):
            def exp(i, r):
                act.wait_ge(sem("gate_in"), i * PARTS + r + 1)
                nc.scalar.activation(gate_exp[r % RING2], gate_z[r % RING2], ACT.Exp).then_inc(sem("gate_exp"), 1)

            def copy(i, r):
                n = i * PARTS + r
                act.wait_ge(sem("gate_turned"), n + 1)
                wait(act, sem("gate_logits"), n - RING2 + 1)
                nc.scalar.activation(hot_t[:, r % RING2], banks(0), ACT.Copy).then_inc(sem("gate_copied"), 1)

            def scale(i, r):
                act.wait_ge(sem("gates_ready"), i * PARTS + r + 1)
                for u in range(U):
                    last = nc.scalar.activation(scaled[:, u, :], rows[:, r * U + u, D:KV], ACT.Copy,
                                                scale=msg_gate[:, r * U + u, GATE2:GATE2 + 1])
                last.then_inc(sem("gate_scaled"), 1)
            edge_loop(act, [(0, step_idx(act, GATE_PASS)), (2, exp), (1, copy), (2, scale)])

        gate_z = [small[:, k, 0:4 * U].rearrange("p (u c) -> p u c", c=4) for k in range(RING2)]
        gate_exp = [small[:, k, 4 * U:8 * U].rearrange("p (u c) -> p u c", c=4) for k in range(RING2)]
        gate_max = [small[:, k, 8 * U:9 * U] for k in range(RING2)]
        gate_sum = [small[:, k, 9 * U:10 * U] for k in range(RING2)]

        def gate_pe(pe):
            def turn(i, r):
                n = i * PARTS + r
                pe.wait_ge(sem("hot_ready"), GATE_HOT0 + n + 1)
                wait(pe, sem("gate_copied"), n)
                for u in range(U):
                    last = nc.tensor.transpose(banks(0)[:, u * P:(u + 1) * P], hot[:, r * U + u, :], ident[:])
                last.then_inc(sem("gate_turned"), 1)

            def logits(i, r):
                n = i * PARTS + r
                blocks = registers(PE, block_row, i, r, BLOCKS - 1)
                pe.wait_ge(sem("gate_copied"), n + 1)
                wait(pe, sem("gate_in"), n - RING2 + 1)
                pe.sem_inc(sem("pe_turn"), 1)
                for u in range(U):
                    last = nc.tensor.matmul(banks(2 + r % RING2)[:, u * 4:u * 4 + 4], hot_t[:, r % RING2, u * P:(u + 1) * P],
                                            logits_dst[:, ds(blocks[u], 1), :].rearrange("p b f -> p (b f)"), start=True, stop=True)
                last.then_inc(sem("gate_logits"), 1)

            def arrived(i, r):
                pe.wait_ge(sem("gate_msg"), i * PARTS + r + 1)
            sums = gate_sums.step_pe(pe, lambda r, u: msg_gate[:, r * U + u, :], arrived)
            edge_loop(pe, [(0, turn), (3, sums), (0, logits)])

        def gate_dve(dve, chain):
            def logits(i, r):
                n, z = i * PARTS + r, gate_z[r % RING2]
                dve.wait_ge(sem("gate_logits"), n + 1)
                dve.wait_ge(rows_in[r], 16 * U * (GATE_TURN0 + i + 1))
                nc.vector.tensor_tensor(z, banks(2 + r % RING2)[:, 0:4 * U].rearrange("p (u c) -> p u c", c=4),
                                        rows[:, r * U:(r + 1) * U, KV:GATE_ROW], ALU.add).then_inc(sem("gate_step"), 1)
                dve.wait_ge(sem("gate_step"), 4 * n + 1)
                nc.vector.tensor_reduce(gate_max[r % RING2], z[:, :, 0:3], AX.X, ALU.max).then_inc(sem("gate_step"), 1)
                dve.wait_ge(sem("gate_step"), 4 * n + 2)
                nc.vector.tensor_tensor(z, z, gate_max[r % RING2].unsqueeze(2).broadcast_to((P, U, 4)),
                                        ALU.subtract).then_inc(sem("gate_in"), 1)

            def gates(i, r):
                n, e = i * PARTS + r, gate_exp[r % RING2]
                dve.wait_ge(sem("gate_exp"), n + 1)
                nc.vector.tensor_reduce(gate_sum[r % RING2], e[:, :, 0:3], AX.X, ALU.add).then_inc(sem("gate_step"), 1)
                dve.wait_ge(sem("gate_step"), 4 * n + 3)
                nc.vector.reciprocal(gate_max[r % RING2], gate_sum[r % RING2]).then_inc(sem("gate_step"), 1)
                dve.wait_ge(sem("gate_step"), 4 * n + 4)
                nc.vector.tensor_tensor(msg_gate[:, r * U:(r + 1) * U, D:D + 3], e[:, :, 0:3],
                                        gate_max[r % RING2].unsqueeze(2).broadcast_to((P, U, 3)), ALU.mult).then_inc(sem("gates_ready"), 1)

            def message(i, r):
                n = i * PARTS + r
                dve.wait_ge(sem("gate_scaled"), n + 1)
                for u in range(U):
                    m = r * U + u
                    last = nc.vector.scalar_tensor_tensor(msg_gate[:, m, 0:D], rows[:, r * U + u, 0:D], msg_gate[:, m, D:D + 1],
                                                          scaled[:, u, :], ALU.mult, ALU.add)
                last.then_inc(sem("gate_msg"), 1)
            chain.after(nc.vector.memset(acc_flat[:, 0:BLOCKS * GATE_W], 0.0))
            chain.after(nc.vector.memset(h_flat[:], 0.0))
            def hot_free(i, r):
                if not isinstance(i, int) or i:
                    dve.wait_ge(sem("win_done"), gate_sums.done0 + U * ((i - 1) * PARTS + r + 1))
            chain.after(nc.vector.memset(msg_gate[:, :, GATE_W - 1:GATE_W], 0.0))
            gate_sums.start(dve)
            edge_loop(dve, [(2, logits), (3, message), (2, gates), (0, step_hot(hot_free)), (4, gate_sums.step_add(dve))])
            gate_sums.end(dve)
            chain.after(nc.vector.tensor_tensor(acc_flat[:, 0:BLOCKS * GATE_W], acc_flat[:, 0:BLOCKS * GATE_W], h_flat[:], ALU.add))
            sums = by_block(acc_flat, BLOCKS, GATE_W)
            chain.after(nc.vector.tensor_tensor(t, t, sums[:, :, GATE1:GATE1 + 1].broadcast_to((P, BLOCKS, D)), ALU.mult))
            chain.after(nc.vector.tensor_tensor(w, w, sums[:, :, GATE2:GATE2 + 1].broadcast_to((P, BLOCKS, D)), ALU.mult))
            chain.after(nc.vector.tensor_tensor(x, x, sums[:, :, 0:D], ALU.add))
            chain.after(nc.vector.tensor_tensor(x, x, t, ALU.add))
            chain.after(nc.vector.tensor_tensor(x, x, w, ALU.add))

        L0_B1, B_SRC, B_DST, B_EDGE = range(4)
        derived = banks(6)

        def derived_pe(pe):
            pe.wait_ge(sem("weights_in"), 16 * 7)
            pe.wait_ge(sem("bias_wide"), 1)
            def product(at, n, pairs):
                for k, (left, right) in enumerate(pairs):
                    ins = nc.tensor.matmul(derived[:, at:at + n], left, right, start=k == 0, stop=k == len(pairs) - 1)
                return ins
            gate = [w_gate[:, k, :] for k in range(3)]
            product(0, D, [(weight("L0_w1"), weight("L0_w2t"))])
            product(D, D, [(bias_wide[:, L0_B1], weight("L0_w2t"))])
            product(2 * D, 3, [(weight("L3_Wsrc_t"), gate[0]), (weight("L3_Wedge_src_t"), gate[2])])
            product(2 * D + 4, 3, [(weight("L3_Wdst_t"), gate[1]), (weight("L3_Wedge_dst_t"), gate[2])])
            product(2 * D + 8, 3, [(bias_wide[:, B_SRC], gate[0])])
            product(2 * D + 12, 3, [(bias_wide[:, B_DST], gate[1]), (bias_wide[:, B_EDGE], gate[2])]).then_inc(sem("derived"), 1)

        def derived_dve(dve, chain):
            dve.wait_ge(sem("weights_in"), 16 * 7)
            nc.vector.tensor_copy(bias_wide, bias_cols[:].unsqueeze(2).broadcast_to((P, 4, D))).then_inc(sem("bias_wide"), 1)
            chain.after(nc.vector.memset(w_logit[:], 0.0))
            chain.after(nc.vector.memset(b_logit[:], 0.0))

            def add(into, other, op=ALU.add):
                target = biases[:, BIASES.index(into), :]
                chain.after(nc.vector.tensor_tensor(target, target, biases_once[:, BIASES_ONCE.index(other), :], op))
            add("L2_bn1", "L2_bs1")
            add("L2_bn2", "L2_bs2")
            add("L1_Wbeta_out", "L1_Wbeta_diff")
            add("L1_Wbeta_skip", "L1_Wbeta_diff", ALU.subtract)
            dve.wait_ge(sem("derived"), 1)
            chain.after(nc.vector.tensor_copy(weight("L0_w1"), derived[:, 0:D]))
            chain.after(nc.vector.tensor_tensor(biases[:, BIASES.index("L0_b2"), :], biases[:, BIASES.index("L0_b2"), :], derived[:, D:2 * D], ALU.add))
            for k in range(2):
                chain.after(nc.vector.tensor_copy(w_logit[:, 4 * k:4 * k + 3], derived[:, 2 * D + 4 * k:2 * D + 4 * k + 3]))
                chain.after(nc.vector.tensor_copy(b_logit[:, 4 * k:4 * k + 3], derived[:, 2 * D + 8 + 4 * k:2 * D + 8 + 4 * k + 3]))
            chain.after(nc.vector.tensor_tensor(b_logit[:, 4:7], b_logit[:, 4:7], b_gate[:], ALU.add))

        @block.sync
        def _(sp):
            sp.dma_start(tile_ends[:, 0, :], a["tile_first"].partition_broadcast(P)).then_inc(sem("ends_in"), 16)
            sp.dma_start(tile_ends[:, 1, :], a["tile_last"].partition_broadcast(P)).then_inc(sem("ends_in"), 16)
            sp.dma_start(dst_cols[:, 0:TILES], a["dst_cols"]).then_inc(sem("cols_in"), 16)
            sp.dma_start(x[:, 0:BLOCKS - 1, :], a["x"][0:NODES - TAIL, :].rearrange("(b p) f -> p b f", p=P)).then_inc(sem("x_in"), 16)
            sp.wait_ge(sem("x_zeroed"), 1)
            sp.dma_start(x[0:TAIL, BLOCKS - 1, :], a["x"][NODES - TAIL:NODES, :]).then_inc(sem("x_in"), 16)
            with nc.allow_non_contiguous_dma(reason="short rows, once"):
                sp.dma_start(weights[:], a["weights"]).then_inc(sem("weights_in"), 16)
                sp.dma_start(biases[:].rearrange("p n f -> p (n f)"), a["biases"].rearrange("n f -> (n f)").partition_broadcast(P)).then_inc(sem("weights_in"), 16)
                sp.dma_start(weights_once, a["weights_once"]).then_inc(sem("weights_in"), 16)
                sp.dma_start(biases_once.rearrange("p n f -> p (n f)"), a["biases_once"].rearrange("n f -> (n f)").partition_broadcast(P)).then_inc(sem("weights_in"), 16)
                sp.dma_start(bias_cols[:], a["bias_cols"]).then_inc(sem("weights_in"), 16)
                sp.dma_start(w_gate[:], a["w_gate"].rearrange("(k p) c -> p k c", p=P)).then_inc(sem("weights_in"), 16)
                sp.dma_start(b_gate[:], a["b_gate"].partition_broadcast(P)).then_inc(sem("weights_in"), 16)
            sp.wait_ge(sem("step_tables"), 1)
            with nc.allow_non_contiguous_dma(reason="small tables, once"):
                sp.dma_start(d_block.rearrange("(c p) -> p c", p=P), step_i[:, 1, :]).then_inc(sem("tables_out"), 16)
                sp.dma_start(d_row0.rearrange("(c p) -> p c", p=P), step_i[:, 2, :]).then_inc(sem("tables_out"), 16)
                sp.wait_ge(sem("tables_out"), 32)
                sp.dma_start(block_row, d_block.rearrange("(o n) -> o n", o=1)).then_inc(sem("window_in"), 16)
                sp.dma_start(row0_row, d_row0.rearrange("(o n) -> o n", o=1)).then_inc(sem("window_in"), 16)
                sp.wait_ge(sem("step_rows"), 16 * 2 * CHUNKS)
                sp.wait_ge(sem("before_first"), 1)
                sp.dma_start(before[1:P, :], edge_i[0:P - 1, 0:CHUNKS, P - 1]).then_inc(sem("before_in"), 16)
                sp.dma_start(before[0:1, 1:CHUNKS], edge_i[P - 1:P, 0:CHUNKS - 1, P - 1]).then_inc(sem("before_in"), 16)
            sp.wait_ge(sem("rel_rows"), 1)
            sp.dma_start(d_reset.rearrange("(c p) e -> p c e", p=P), edge_f[RESET]).then_inc(sem("reset_out"), 16)

            def table(j):
                sp.wait_ge(sem("t_ready"), j + 1)
                sp.dma_start(node_rows(tab_lin[j]), t).then_inc(sem("table_out"), 16)
            table(0)
            table(1)
            sp.wait_ge(sem("window_in"), 32)
            sp.wait_ge(sem("kv_ready"), 1)
            sp.dma_start(node_rows(tab_kv)[:, :, 0:D], acc).then_inc(sem("table_out"), 16)
            sp.dma_start(node_rows(tab_kv)[:, :, D:KV], w).then_inc(sem("table_out"), 16)
            sp.wait_ge(sem("table_out"), KV_TABLE)
            sp.wait_ge(sem("reset_out"), 16)
            max_sp(sp)
            att_sp(sp)
            sums_sp(sp)
            sp.wait_ge(sem("t_ready"), 3)
            sp.dma_start(node_rows(tab_lin[2]), h).then_inc(sem("table_out"), 16)
            table(3)
            sp.wait_ge(sem("gate_table"), 1)
            with nc.allow_non_contiguous_dma(reason="four logits of each node"):
                sp.dma_start(node_rows(tab_gate)[:, :, 0:D], acc).then_inc(sem("table_out"), 16)
                sp.dma_start(node_rows(tab_gate)[:, :, D:KV], h).then_inc(sem("table_out"), 16)
                sp.dma_start(node_rows(tab_gate)[:, :, KV:GATE_ROW], logits_src[:]).then_inc(sem("table_out"), 16)
            sp.wait_ge(sem("out_ready"), 1)
            sp.dma_start(out[0:NODES - TAIL, :].rearrange("(b p) f -> p b f", p=P), x[:, 0:BLOCKS - 1, :]).then_inc(sem("stored"), 16)
            sp.dma_start(out[NODES - TAIL:NODES, :], x[0:TAIL, BLOCKS - 1, :]).then_inc(sem("stored"), 16)
            sp.wait_ge(sem("stored"), 32)
            sp.wait_ge(sem("reset_out"), 16)

        @block.gpsimd
        def _(pool):
            pool.memset(x[:, BLOCKS - 1, :], 0.0).then_inc(sem("x_zeroed"), 1)
            pool.memset(dst_cols[:, TILES:HIST_PAD], -1).then_inc(sem("cols_zeroed"), 1)
            pool.memset(before[0:1, 0:1], -2).then_inc(sem("before_first"), 1)
            pool.iota(iota[:], [[1, P]], base=0, channel_multiplier=0,
                      allow_small_or_imprecise_dtypes=True).then_inc(sem("consts"), 1)
            pool.iota(iota_bf[:], [[1, P]], base=0, channel_multiplier=0,
                      allow_small_or_imprecise_dtypes=True).then_inc(sem("consts"), 1)
            pool.iota(step_no[:], [[P, CHUNKS]], base=0, channel_multiplier=1,
                      allow_small_or_imprecise_dtypes=True).then_inc(sem("consts"), 1)
            pool.memset(ident[:], 0.0).then_inc(sem("consts"), 1)
            pool.wait_ge(sem("consts"), 4)
            pool.affine_select(out=ident[:], in_=ident[:], compare_op=ALU.not_equal, fill=1.0, base=0,
                               pattern=[[-1, P]], channel_multiplier=1).then_inc(sem("consts"), 1)
            pool.wait_ge(sem("step_tables"), 1)
            for c in range(CHUNKS):
                for k, tiles in enumerate((a["dst_tiles"], a["src_tiles"])):
                    pool.indirect_dma_start(edge_i[:, k * CHUNKS + c, :], None, tiles,
                                            bass.IndirectOffsetOnAxis(step_i[:, 0, c:c + 1], 0)).then_inc(sem("step_rows"), 16)
            lin_pool(pool, 0)
            lin_pool(pool, 1)
            att_pool(pool)
            sums_pool(pool)
            lin_pool(pool, 2)
            lin_pool(pool, 3)
            gate_pool(pool)

        @block.scalar
        def _(act):
            norm_act(act, 0)
            root_act(act, 0)
            root_act(act, 1)
            act.wait_ge(sem("cols_ready"), 1)
            lin_act(act, 0)
            lin_act(act, 1)
            p_l0.act(act)
            norm_act(act, 1)
            root_act(act, 2)
            p_qkv.act(act)
            att_act(act)
            turn_act(act, 0)
            turn_act(act, 1)
            sums_act(act)
            p_skip.act(act)
            beta_act(act)
            norm_act(act, 2)
            root_act(act, 3)
            norm_act(act, 3)
            root_act(act, 4)
            lin_act(act, 2)
            p_sage1.act(act)
            lin_act(act, 3)
            p_sage2.act(act)
            norm_act(act, 4)
            root_act(act, 5)
            p_gate.act(act)
            gate_act(act)

        @block.tensor
        def _(pe):
            def hist(n, p, first, last):
                pe.wait_ge(sem("hist_hot"), n + 1)
                for j in range(HIST_TILES):
                    ins = nc.tensor.matmul(banks(7)[:, 0:BLOCKS], hot_lo[p][:, j, :], hot_hi[p][:, j, :],
                                           start=first and j == 0, stop=last and j == HIST_TILES - 1, skip_group_check=True)
                ins.then_inc(sem("hist_done"), 1)
            hist(0, 0, True, False)
            hist(1, 1, False, False)
            with pe.Fori(1, HIST_TURNS - 1) as i:
                hist(2 * i, 0, False, False)
                hist(2 * i + 1, 1, False, False)
            hist(2 * HIST_TURNS - 2, 0, False, False)
            hist(2 * HIST_TURNS - 1, 1, False, True)
            pe.wait_ge(sem("consts"), 5)
            pe.wait_ge(sem("rel_rows"), 1)
            for n, k in enumerate((REL, SRC)):
                for c in range(CHUNKS):
                    at = (n * CHUNKS + c) * P
                    last = nc.tensor.transpose(ps[:, at:at + P], edge_f[k][:, c, :], ident[:])
            last.then_inc(sem("rows_t"), 1)
            derived_pe(pe)
            pe.wait_ge(sem("cols_ready"), 1)
            lin_pe(pe, 0)
            lin_pe(pe, 1)
            p_l0.pe(pe)
            p_qkv.pe(pe)
            pe.wait_ge(sem("kv_ready"), 1)
            att_pe(pe)
            turn_pe(pe, 0)
            carry_pe(pe, 0)
            carry_pe(pe, 1)
            turn_pe(pe, 1)
            sums_pe(pe)
            p_skip.pe(pe)
            lin_pe(pe, 2)
            p_sage1.pe(pe)
            lin_pe(pe, 3)
            p_sage2.pe(pe)
            p_gate.pe(pe)
            gate_pe(pe)

        @block.vector
        def _(dve):
            chain = Chain(dve, sem("dve_chain"))
            dve.wait_ge(sem("ends_in"), 32)
            dve.wait_ge(sem("consts"), 5)
            nc.vector.memset(setup[:, 3, :], 0.0)
            chain.after(nc.vector.tensor_scalar(blk, tile_ends, 7, None, ALU.arith_shift_right))
            chain.after(nc.vector.tensor_copy(setup[:, 0, :], blk[:, 0, :]))
            chain.after(nc.vector.tensor_tensor(tile_ends[:, 0, :], blk[:, 1, :], blk[:, 0, :], ALU.subtract))
            chain.after(nc.vector.tensor_scalar(setup[:, 1, :], tile_ends[:, 0, :], 1.0, None, ALU.add))
            chain.after(nc.vector.tensor_tensor_scan(setup[:, 2, :], setup[:, 1, :], setup[:, 3, :], 0.0, ALU.add, ALU.add))
            chain.after(nc.vector.tensor_tensor(setup[:, 2, :], setup[:, 2, :], setup[:, 1, :], ALU.subtract))
            chain.after(nc.vector.tensor_tensor(setup[:, 4, :], setup[:, 0, :], setup[:, 2, :], ALU.subtract))
            chain.after(nc.vector.tensor_copy(setup[:, 5, 0:1], setup[:, 4, 0:1]))
            chain.after(nc.vector.tensor_tensor(setup[:, 5, 1:TILES], setup[:, 4, 1:TILES], setup[:, 4, 0:TILES - 1], ALU.subtract))
            for c in range(CHUNKS):
                chain.after(nc.vector.tensor_scalar(setup[:, 3, :], setup[:, 2, :], step_no[:, c:c + 1], None, ALU.is_le, ALU.add,
                                                    accum_out=step_f[:, 0, c:c + 1]))
                chain.after(nc.vector.scalar_tensor_tensor(setup[:, 1, :], setup[:, 2, :], step_no[:, c:c + 1], setup[:, 5, :],
                                                           ALU.is_le, ALU.mult, accum_out=step_f[:, 1, c:c + 1]))
            chain.after(nc.vector.tensor_tensor(step_f[:, 2, :], step_no[:], step_f[:, 1, :], ALU.add))
            chain.after(nc.vector.tensor_scalar(step_f[:, 3, :], step_f[:, 2, :], float(P), None, ALU.mult))
            nc.vector.tensor_scalar(step_i[:, 0, :], step_f[:, 0, :], -1.0, None, ALU.add)
            nc.vector.tensor_scalar(step_i[:, 1, :], step_f[:, 2, :], float(BLOCKS - 1), None, ALU.min)
            nc.vector.tensor_scalar(step_i[:, 2, :], step_f[:, 0, :], float(P), -float(P), ALU.mult, ALU.add).then_inc(sem("step_tables"), 1)
            dve.wait_ge(sem("cols_zeroed"), 1)
            dve.wait_ge(sem("cols_in"), 16)
            nc.vector.tensor_scalar(lohi_i[:, 0, :], dst_cols, P - 1, None, ALU.bitwise_and)
            chain.after(nc.vector.tensor_scalar(lohi_i[:, 1, :], dst_cols, 7, None, ALU.arith_shift_right))
            chain.after(nc.vector.tensor_copy(lohi, lohi_i))

            def hist(i, p, first):
                n = 2 * i + p
                if not first:
                    dve.wait_ge(sem("hist_done"), n - 1)
                at = ds(n * HIST_TILES, HIST_TILES)
                nc.vector.tensor_tensor(hot_lo[p], iota_bf[:].unsqueeze(1).broadcast_to((P, HIST_TILES, P)),
                                        lohi[:, 0, at].unsqueeze(2).broadcast_to((P, HIST_TILES, P)), ALU.is_equal)
                nc.vector.tensor_tensor(hot_hi[p], iota_bf[:, 0:BLOCKS].unsqueeze(1).broadcast_to((P, HIST_TILES, BLOCKS)),
                                        lohi[:, 1, at].unsqueeze(2).broadcast_to((P, HIST_TILES, BLOCKS)),
                                        ALU.is_equal).then_inc(sem("hist_hot"), 1)
            hist(0, 0, True)
            hist(0, 1, True)
            with dve.Fori(1, HIST_TURNS) as i:
                hist(i, 0, False)
                hist(i, 1, False)
            dve.wait_ge(sem("step_rows"), 16 * 2 * CHUNKS)
            dve.wait_ge(sem("before_in"), 32)
            dve.wait_ge(sem("before_first"), 1)
            dst_i = edge_i[:, 0:CHUNKS, :]
            base = step_f[:, 3, :].unsqueeze(2).broadcast_to((P, CHUNKS, P))
            chain.after(nc.vector.tensor_copy(edge_f[LAST], dst_i))
            chain.after(nc.vector.tensor_copy(step_f[:, 4, :], before[:]))
            chain.after(nc.vector.tensor_tensor(edge_f[REL], edge_f[LAST], base, ALU.subtract))
            nc.vector.tensor_copy(edge_f[SRC], edge_i[:, CHUNKS:2 * CHUNKS, :])
            nc.vector.tensor_tensor(edge_f[RESET][:, :, 1:P], edge_f[LAST][:, :, 1:P], edge_f[LAST][:, :, 0:P - 1], ALU.not_equal)
            chain.after(nc.vector.tensor_tensor(edge_f[RESET][:, :, 0], edge_f[LAST][:, :, 0], step_f[:, 4, :], ALU.not_equal))
            nc.vector.tensor_scalar(edge_f[RESET], edge_f[RESET], -BIG, None, ALU.mult).then_inc(sem("rel_rows"), 1)
            dve.wait_ge(sem("rows_t"), 1)
            nc.vector.tensor_copy(rel_col[:], ps[:, 0:STEP_PAD])
            nc.vector.tensor_copy(src_col[:], ps[:, STEP_PAD:2 * STEP_PAD]).then_inc(sem("cols_ready"), 1)
            dve.wait_ge(sem("cols_ready"), 1)
            derived_dve(dve, chain)
            dve.wait_ge(sem("window_in"), 32)
            dve.wait_ge(sem("reset_out"), 16)
            dve.wait_ge(sem("x_in"), 32)
            norm_relu_dve(dve, chain, 0, 0)
            dve.wait_ge(sem("hist_done"), 2 * HIST_TURNS)
            deg = banks(7)[:, 0:BLOCKS]
            chain.after(nc.vector.tensor_scalar(inv_deg[:], deg, 1.0, None, ALU.max))
            chain.after(nc.vector.reciprocal(inv_deg[:], inv_deg[:]))
            nc.vector.tensor_scalar(stat[:, 3, :], deg, 1.0, None, ALU.add).then_inc(sem("var_ready"), 1)
            rsqrt_dve(dve, chain, 1, dinv[:])
            chain.after(nc.vector.tensor_scalar(half_dinv[:], dinv[:], 0.5, None, ALU.mult))
            nc.vector.tensor_tensor(t, h, by_node(dinv[:]), ALU.mult).then_inc(sem("t_ready"), 1)
            dve.wait_ge(sem("t_ready"), 1)
            for j in range(2):
                lin_dve(dve, chain, j)
                chain.after(nc.vector.tensor_tensor(w, acc, t, ALU.add))
                chain.after(nc.vector.tensor_tensor(w, w, by_node(dinv[:]), ALU.mult))
                chain.after(nc.vector.tensor_tensor(w, w, h, ALU.add))
                if j == 0:
                    dve.wait_ge(sem("table_out"), LIN_TABLES[0])
                    nc.vector.tensor_tensor(t, w, by_node(half_dinv[:]), ALU.mult).then_inc(sem("t_ready"), 1)
                    dve.wait_ge(sem("t_ready"), 2)
            chain.after(nc.vector.tensor_scalar(w, w, 0.5, 0.0, ALU.mult, ALU.max))
            p_l0.dve(dve)
            norm_relu_dve(dve, chain, 1, 2)
            dve.wait_ge(sem("table_out"), LIN_TABLES[1])
            p_qkv.dve(dve)
            chain.after(nc.vector.tensor_scalar(t, t, 1.0 / HEAD_DIM ** 0.5, None, ALU.mult))
            dve.sem_inc(sem("kv_ready"), 1)
            att_dve(dve)
            max_dve(dve, chain)
            sums_dve(dve, chain)
            att_end_dve(dve, chain)
            norm_relu_dve(dve, chain, 3, 4)
            dve.sem_inc(sem("t_ready"), 1)
            lin_dve(dve, chain, 2)
            chain.after(nc.vector.tensor_tensor(w, acc, by_node(inv_deg[:]), ALU.mult))
            p_sage1.dve(dve)
            dve.sem_inc(sem("t_ready"), 1)
            lin_dve(dve, chain, 3)
            chain.after(nc.vector.tensor_tensor(w, acc, by_node(inv_deg[:]), ALU.mult))
            p_sage2.dve(dve)
            norm_relu_dve(dve, chain, 4, 5)
            p_gate.dve(dve)
            dve.sem_inc(sem("gate_table"), 1)
            dve.wait_ge(sem("table_out"), GATE_TABLE)
            gate_dve(dve, chain)
            dve.sem_inc(sem("out_ready"), 1)


def kernel(**inputs):
    import concourse.bacc as bacc
    from concourse.bass_utils import run_bass_kernel_spmd as run

    v = {n.replace("_gnn", ""): np.asarray(array) for n, array in inputs.items()}
    src, dst, attr = v["src"], v["dst"], v["edge_attr_128"]
    pad = TILES * P - EDGES
    dst_tiles = np.concatenate([dst, np.full(pad, -1, dst.dtype)]).reshape(TILES, P)
    src_tiles = np.concatenate([src, np.zeros(pad, src.dtype)]).reshape(TILES, P)
    stacked = {"L0_w1": v["L0_w1"], "L0_w2t": v["L0_w2"].T, "L1_Wq": v["L1_Wq"], "L1_Wk": v["L1_Wk"], "L1_Wv": v["L1_Wv"],
               "L1_We": v["L1_We"], "L1_Wskip": v["L1_Wskip"], "L2_Wn1t": v["L2_W_neigh1"].T, "L2_Ws1t": v["L2_W_self1"].T,
               "L2_Wn2t": v["L2_W_neigh2"].T, "L2_Ws2t": v["L2_W_self2"].T, "L3_Wsrc": v["L3_W_src"], "L3_Wdst": v["L3_W_dst"],
               "L3_Wedge_src": v["L3_W_edge"][0:D], "L3_Wedge_dst": v["L3_W_edge"][D:2 * D], "L3_Wsrc_t": v["L3_W_src"].T,
               "L3_Wdst_t": v["L3_W_dst"].T, "L3_Wedge_src_t": v["L3_W_edge"][0:D].T, "L3_Wedge_dst_t": v["L3_W_edge"][D:2 * D].T}
    wbeta = v["L1_Wbeta"].reshape(3, D)
    rows = {"L1_gamma": v["L1_ln_gamma"], "L1_beta": v["L1_ln_beta"], "L1_Wbeta_out": wbeta[0], "L1_Wbeta_skip": wbeta[1],
            "L1_Wbeta_diff": wbeta[2], "L2_bn1": v["L2_b_neigh1"], "L2_bs1": v["L2_b_self1"],
            "L2_bn2": v["L2_b_neigh2"], "L2_bs2": v["L2_b_self2"]}
    arrays = {
        "x": v["x"],
        "attr": np.concatenate([attr, np.zeros((pad, D), attr.dtype)]),
        "dst_tiles": dst_tiles,
        "dst_cols": dst_tiles.T,
        "src_tiles": src_tiles,
        "tile_first": dst[0::P],
        "tile_last": np.concatenate([dst[P - 1::P], dst[EDGES - 1:]]),
        "weights": np.stack([stacked[n] for n in WEIGHTS], axis=1),
        "weights_once": np.stack([stacked[n] for n in WEIGHTS_ONCE], axis=1),
        "biases": np.stack([rows[n] if n in rows else v[n] for n in BIASES]),
        "biases_once": np.stack([rows[n] for n in BIASES_ONCE]),
        "bias_cols": np.stack([v["L0_b1"], v["L3_b_src"], v["L3_b_dst"], v["L3_b_edge"]], axis=1),
        "w_gate": v["L3_W_gate"],
        "b_gate": v["L3_b_gate"],
    }
    arrays = {n: np.ascontiguousarray(v) for n, v in arrays.items()}
    nc = bacc.Bacc("TRN2", target_bir_lowering=False, num_devices=1)
    a = {n: nc.dram_tensor(n + "_dram", v.shape, mybir.dt.from_np(v.dtype), kind="ExternalInput").ap() for n, v in arrays.items()}
    out = nc.dram_tensor("out_dram", (NODES, D), mybir.dt.float32, kind="ExternalOutput").ap()
    program(nc, a, out)
    r = run(nc, [{n + "_dram": v for n, v in arrays.items()}], core_ids=[0])
    return r.results[0]["out_dram"]
```
